# Optimizing a Trainium2 kernel written in Bass

```python
import numpy as np
import jax
import jax.numpy as jnp

def _softmax(x, axis=-1):
    return jax.nn.softmax(x, axis=axis)
def _gelu(x):
    return jax.nn.gelu(x, approximate=True)
def _silu(x):
    return jax.nn.silu(x)
def _sigmoid(x):
    return jax.nn.sigmoid(x)
def _layernorm(x, axis=-1, eps=1e-5):
    m = jnp.mean(x, axis=axis, keepdims=True)
    v = jnp.var(x, axis=axis, keepdims=True)
    return (x - m) / jnp.sqrt(v + eps)
def _scatter_add(tgt, idx, src, axis=0):
    return tgt.at[idx].add(src)
def _segment_sum(src, seg, n):
    return jax.ops.segment_sum(src, seg, n)

kernel_name = 'mk_adj_resnorm_d1_adj_128_79b7ce'

def setup_inputs(seed: int = 0):
    np.random.seed(seed)
    _w = jnp.asarray
    def _rec_inputs():
        import jax
        import jax.numpy as jnp
        _gk = jax.random.key(seed)
        x = -0.001003 + 1 * jax.random.normal(jax.random.fold_in(_gk, 1), (8192, 128), jnp.float32)
        _w = (1.0 + jnp.arange(8192, dtype=jnp.float32)) ** -0.5
        _w = _w / _w.mean()
        _pij = jnp.clip(0.000488281 * _w[:, None] * _w[None, :], 0.0, 1.0)
        _a = jax.random.uniform(jax.random.fold_in(_gk, 2), (8192, 8192)) < _pij
        _a = jnp.logical_or(_a, jnp.swapaxes(_a, -1, -2))
        _a = jnp.logical_or(_a, jnp.eye(8192, dtype=bool))
        _af = _a.astype(jnp.float32)
        _af = _af * jax.random.uniform(jax.random.fold_in(_gk, 3), (8192, 8192), jnp.float32, 0.05, 5.41998)
        adj = _af
        return x, adj
    x, adj = _rec_inputs()
    def _L0_gnn_setup():
        import jax, jax.numpy as jnp
        import numpy as np
        N = 12288
        F_IN = 128
        F_OUT = 128
        key = jax.random.key(seed)
        k1, k2, k3, k4, k5, k6, k7 = jax.random.split(key, 7)
        stdv = 1.0 / np.sqrt(F_OUT)
        return {'feats': jax.random.normal(k1, (N, F_IN), dtype=jnp.float32), 'node_adj': jax.random.normal(k2, (N, N), dtype=jnp.float32), 'edge_adj': jax.random.normal(k3, (N, N), dtype=jnp.float32), 'node_weight': jax.random.uniform(k4, (2 * F_IN, F_OUT), dtype=jnp.float32, minval=-stdv, maxval=stdv), 'node_bias': jax.random.uniform(k5, (F_OUT,), dtype=jnp.float32, minval=-stdv, maxval=stdv), 'edge_weight': jax.random.uniform(k6, (F_IN, F_OUT), dtype=jnp.float32, minval=-stdv, maxval=stdv), 'edge_bias': jax.random.uniform(k7, (F_OUT,), dtype=jnp.float32, minval=-stdv, maxval=stdv)}
    _L0_gnn_all = _L0_gnn_setup()
    _L0_gnn_in = {k: v for k, v in _L0_gnn_all.items() if k in ('node_weight', 'node_bias', 'edge_weight', 'edge_bias', )}
    del _L0_gnn_all

    return {
        "x": x,
        "adj": adj,
        "L0_gnn_node_weight": _L0_gnn_in["node_weight"],
        "L0_gnn_node_bias": _L0_gnn_in["node_bias"],
        "L0_gnn_edge_weight": _L0_gnn_in["edge_weight"],
        "L0_gnn_edge_bias": _L0_gnn_in["edge_bias"],
    }

def reference(x, adj, L0_gnn_node_weight, L0_gnn_node_bias, L0_gnn_edge_weight, L0_gnn_edge_bias):
    import jax
    import jax.numpy as jnp
    def _L0_gnn_ref(feats, node_adj, edge_adj, node_weight, node_bias, edge_weight, edge_bias):
        import jax, jax.numpy as jnp
        import numpy as np
        N = 12288
        F_IN = 128
        F_OUT = 128
        pos = (node_adj > 0).astype(feats.dtype)
        neg = (node_adj < 0).astype(feats.dtype)
        node_support = jnp.concatenate([pos @ feats, neg @ feats], axis=1)
        node_output = node_support @ node_weight + node_bias
        edge_support = edge_adj @ feats
        edge_output = edge_support @ edge_weight + edge_bias
        return jax.nn.relu(node_output) + edge_output

    x = _layernorm(x + _L0_gnn_ref(x, adj, adj, L0_gnn_node_weight, L0_gnn_node_bias, L0_gnn_edge_weight, L0_gnn_edge_bias), axis=-1)
    return x


_drawn_inputs = setup_inputs


def setup_inputs(seed=0):
    import zlib

    import numpy as np

    out = dict(_drawn_inputs(seed))
    spreads = {}
    factors = {'L0_gnn_node_bias': 6.535, 'L0_gnn_edge_bias': 4.537}
    for name, (base, spread) in spreads.items():
        noise = np.random.default_rng([zlib.crc32(name.encode()), seed]).standard_normal(out[name].shape)
        drawn = base * np.exp(spread * noise) if base else spread * noise
        out[name] = jnp.asarray(drawn.astype(out[name].dtype))
    for name, factor in factors.items():
        out[name] = (out[name] * factor).astype(out[name].dtype)
    return out
```

```python
from contextlib import ExitStack

import numpy as np

import concourse.bass as bass
from concourse import mybir

F32 = mybir.dt.float32
F32R = mybir.dt.float32r
BF16 = mybir.dt.bfloat16
I32 = mybir.dt.int32
ALU = mybir.AluOpType
ACT = mybir.ActivationFunctionType
AX = mybir.AxisListType

P = 128
COLS = 512
TILES = 4
WIDE = TILES * COLS
RAW_RING = 4
SPLIT_RING = 4
POS_RING = 2
EPS = 1e-5
NEG_SCALE = -(2.0 ** 64)

X_ROWS, NODE_BIASED, EDGE_BIASED, EDGE_ADDED, RESIDUAL_ADDED, STATS, MEAN_VAR, RSTD, NORMED = range(1, 10)
EPI_STEPS = NORMED

PROJECT_AT, SUM_AT, STATS_AT, SQRT_AT, NORM_AT, STORE_AT = 1, 5, 6, 7, 8, 13


def adj_resnorm(nc, adj, x, w_node, b_node, w_edge, b_edge, out):
    BLOCKS, UNITS = adj.shape[0], adj.shape[1]
    F = w_edge.shape[0]
    SUBS = COLS // P
    X_LOADS = x.shape[1] // WIDE
    X_TILES = WIDE // F
    ROUNDS = UNITS // RAW_RING
    assert X_LOADS == RAW_RING and SUBS * F == COLS
    assert UNITS % RAW_RING == 0 and UNITS % SPLIT_RING == 0 and UNITS % POS_RING == 0

    with ExitStack() as stack:
        def sbuf(name, shape, dtype):
            return stack.enter_context(nc.sbuf_tensor(name, shape, dtype))

        def psum(name, shape, dtype):
            return stack.enter_context(nc.psum_tensor(name, shape, dtype))

        def semaphore(name):
            return stack.enter_context(nc.semaphore(name))

        x_hi = sbuf("x_hi", [P, x.shape[1]], F32R)
        x_lo = sbuf("x_lo", [P, x.shape[1]], F32R)
        raw = sbuf("raw", [P, RAW_RING, WIDE], F32)
        adj_hi = sbuf("adj_hi", [P, SPLIT_RING, WIDE], F32R)
        adj_lo = sbuf("adj_lo", [P, SPLIT_RING, WIDE], F32R)
        pos = sbuf("pos", [P, POS_RING, WIDE], F32R)
        neg = sbuf("neg", [P, WIDE], F32R)
        relu_out = sbuf("relu_out", [P, 2, WIDE], BF16)
        neg_sums = sbuf("neg_sums", [P, BLOCKS * UNITS], F32)
        neg_total = sbuf("neg_total", [P, 1], F32)
        ones = sbuf("ones", [P, 1], F32)
        none_negative = sbuf("none_negative", [1, 1], I32)
        pos_support = sbuf("pos_support", [P, COLS], F32)
        neg_support = sbuf("neg_support", [P, COLS], F32)
        edge_support = sbuf("edge_support", [P, COLS], F32)
        w_pos_sb = sbuf("w_pos_sb", [P, F], F32)
        w_neg_sb = sbuf("w_neg_sb", [P, F], F32)
        w_edge_sb = sbuf("w_edge_sb", [P, F], F32)
        b_node_sb = sbuf("b_node_sb", [P, F], F32)
        b_edge_sb = sbuf("b_edge_sb", [P, F], F32)
        eps_sb = sbuf("eps_sb", [P, 1], F32)
        x_rows = sbuf("x_rows", [P, SUBS, F], F32)
        summed = sbuf("summed", [P, SUBS, F], F32)
        normed = sbuf("normed", [P, SUBS, F], F32)
        stats = sbuf("stats", [P, SUBS, 6], F32)
        mean_var = sbuf("mean_var", [P, SUBS, 2], F32)
        std = sbuf("std", [P, SUBS], F32)
        rstd = sbuf("rstd", [P, SUBS], F32)
        pos_ps = psum("pos_ps", [P, COLS], F32)
        neg_ps = psum("neg_ps", [P, COLS], F32)
        edge_ps = psum("edge_ps", [P, COLS], F32)
        node_out_ps = psum("node_out_ps", [P, SUBS, F], F32)
        edge_out_ps = psum("edge_out_ps", [P, SUBS, F], F32)
        total_ps = psum("total_ps", [1, 1], F32)
        raw_loaded = [semaphore(f"raw_loaded_{slot}") for slot in range(RAW_RING)]
        weights_loaded = semaphore("weights_loaded")
        constants_set = semaphore("constants_set")
        hi_ready = semaphore("hi_ready")
        lo_ready = semaphore("lo_ready")
        pos_ready = semaphore("pos_ready")
        neg_ready = semaphore("neg_ready")
        pos_used = semaphore("pos_used")
        neg_used = semaphore("neg_used")
        split_used = semaphore("split_used")
        pos_evicted = semaphore("pos_evicted")
        neg_evicted = semaphore("neg_evicted")
        edge_evicted = semaphore("edge_evicted")
        projected = semaphore("projected")
        epi_step = semaphore("epi_step")
        std_ready = semaphore("std_ready")
        stored = semaphore("stored")
        summed_up = semaphore("summed_up")
        total_ready = semaphore("total_ready")
        flag_ready = semaphore("flag_ready")

        block = stack.enter_context(nc.Block())

        def arrived(b, u):
            return b * (16 * ROUNDS) + 16 * (u // RAW_RING + 2)

        def units(b, u):
            return b * UNITS + (u + 1)

        def split(b, u):
            return b * UNITS + (X_LOADS + u + 1)

        def step(b, s):
            return b * EPI_STEPS + s

        def tile(t):
            return slice(t * COLS, (t + 1) * COLS)

        def x_tile(xs, u, t):
            k = u * TILES + t
            return xs[:, k * F:(k + 1) * F]

        @block.sync
        def _(sp):
            def load_unit(b, src, u):
                sp.wait_ge(lo_ready, units(b, u))
                sp.dma_start(raw[:, u % RAW_RING], adj[src, u]).then_inc(raw_loaded[u % RAW_RING], 16)

            def store_block(b, dst):
                sp.wait_ge(epi_step, step(b, NORMED))
                sp.dma_start(out[dst], normed[:].rearrange("p s f -> p (s f)")).then_inc(stored, 16)

            for n in range(X_LOADS):
                sp.dma_start(raw[:, n], x[:, n * WIDE:(n + 1) * WIDE]).then_inc(raw_loaded[n], 16)
            for u in range(UNITS):
                load_unit(0, 0, u)
            with sp.Fori(1, BLOCKS) as b:
                for u in range(UNITS):
                    load_unit(b, b, u)
                    if u == STORE_AT:
                        store_block(b - 1, b - 1)
            store_block(BLOCKS - 1, BLOCKS - 1)

            sp.wait_ge(flag_ready, 1)
            with sp.If(sp.value_load(none_negative[0:1, 0:1]) == 0):
                with sp.Fori(BLOCKS, 2 * BLOCKS) as b:
                    for u in range(UNITS):
                        load_unit(b, b - BLOCKS, u)
                    store_block(b, b - BLOCKS)
                sp.wait_ge(stored, 2 * BLOCKS * 16)
            with sp.Else():
                sp.wait_ge(stored, BLOCKS * 16)

        @block.gpsimd
        def _(pool):
            pool.dma_start(w_pos_sb[:], w_node[0:F, :]).then_inc(weights_loaded, 16)
            pool.dma_start(w_neg_sb[:], w_node[F:2 * F, :]).then_inc(weights_loaded, 16)
            pool.dma_start(w_edge_sb[:], w_edge).then_inc(weights_loaded, 16)
            pool.dma_start(b_node_sb[:], b_node.partition_broadcast(P)).then_inc(weights_loaded, 16)
            pool.dma_start(b_edge_sb[:], b_edge.partition_broadcast(P)).then_inc(weights_loaded, 16)
            pool.memset(eps_sb[:], EPS).then_inc(constants_set, 1)
            pool.memset(ones[:], 1.0).then_inc(constants_set, 1)

        @block.scalar
        def _(act):
            def add_up_negatives(b, u):
                act.wait_ge(hi_ready, split(b, u - 2))
                act.activation(relu_out[:, u % 2], raw[:, u % RAW_RING], ACT.Relu, scale=NEG_SCALE,
                               accum_out=neg_sums[:, bass.ds(b * UNITS + u, 1)])

            def round_unit(u):
                act.activation(adj_hi[:, u % SPLIT_RING], raw[:, u % RAW_RING], ACT.Copy).then_inc(hi_ready, 1)

            def evict_edge(b):
                act.wait_ge(split_used, units(b, UNITS - 1))
                act.activation(edge_support[:], edge_ps[:], ACT.Copy).then_inc(edge_evicted, 1)

            def sqrt_var(b):
                act.wait_ge(epi_step, step(b, MEAN_VAR))
                act.activation(std[:], mean_var[:, :, 1], ACT.Sqrt, bias=eps_sb[:]).then_inc(std_ready, 1)

            for n in range(X_LOADS):
                act.wait_ge(raw_loaded[n], 16)
                act.activation(x_hi[:, n * WIDE:(n + 1) * WIDE], raw[:, n], ACT.Copy).then_inc(hi_ready, 1)
            act.wait_ge(constants_set, 2)

            for u in range(UNITS):
                act.wait_ge(raw_loaded[u % RAW_RING], arrived(0, u))
                add_up_negatives(0, u)
                if u >= SPLIT_RING:
                    act.wait_ge(split_used, units(0, u - SPLIT_RING))
                round_unit(u)
            with act.Fori(1, BLOCKS) as b:
                for u in range(UNITS):
                    act.wait_ge(raw_loaded[u % RAW_RING], arrived(b, u))
                    add_up_negatives(b, u)
                    if u == SPLIT_RING - 1:
                        evict_edge(b - 1)
                    act.wait_ge(split_used, units(b, u - SPLIT_RING))
                    round_unit(u)
                    if u == SQRT_AT:
                        sqrt_var(b - 1)
            evict_edge(BLOCKS - 1)
            sqrt_var(BLOCKS - 1)

            act.wait_ge(flag_ready, 1)
            with act.If(act.value_load(none_negative[0:1, 0:1]) == 0):
                with act.Fori(BLOCKS, 2 * BLOCKS) as b:
                    for u in range(UNITS):
                        act.wait_ge(raw_loaded[u % RAW_RING], arrived(b, u))
                        act.wait_ge(split_used, units(b, u - SPLIT_RING))
                        round_unit(u)
                    evict_edge(b)
                    sqrt_var(b)

        @block.vector
        def _(dve):
            def mask_positive(u):
                dve.tensor_scalar(pos[:, u % POS_RING], raw[:, u % RAW_RING], 0.0, None, ALU.is_gt).then_inc(pos_ready, 1)

            def mask_negative(u):
                dve.tensor_scalar(neg[:], raw[:, u % RAW_RING], 0.0, None, ALU.is_lt).then_inc(neg_ready, 1)

            def split_unit(b, u):
                dve.wait_ge(hi_ready, split(b, u))
                dve.tensor_tensor(adj_lo[:, u % SPLIT_RING], raw[:, u % RAW_RING],
                                  adj_hi[:, u % SPLIT_RING].bitcast(F32), ALU.subtract).then_inc(lo_ready, 1)

            def evict_pos(b):
                dve.wait_ge(pos_used, units(b, UNITS - 1))
                dve.tensor_copy(pos_support[:], pos_ps[:]).then_inc(pos_evicted, 1)

            def add_up(b, rows):
                dve.tensor_tensor(x_rows[:], x_hi[:, bass.ds(rows * COLS, COLS)].bitcast(F32).rearrange("p (s f) -> p s f", f=F),
                                  x_lo[:, bass.ds(rows * COLS, COLS)].bitcast(F32).rearrange("p (s f) -> p s f", f=F),
                                  ALU.add).then_inc(epi_step, 1)
                dve.wait_ge(projected, b + 1)
                dve.tensor_tensor(summed[:], node_out_ps[:], b_node_sb[:].unsqueeze(1).broadcast_to([P, SUBS, F]),
                                  ALU.add).then_inc(epi_step, 1)
                dve.tensor_tensor(normed[:], edge_out_ps[:], b_edge_sb[:].unsqueeze(1).broadcast_to([P, SUBS, F]),
                                  ALU.add).then_inc(epi_step, 1)
                dve.wait_ge(epi_step, step(b, EDGE_BIASED))
                dve.scalar_tensor_tensor(summed[:], summed[:], 0.0, normed[:], ALU.max, ALU.add).then_inc(epi_step, 1)
                dve.wait_ge(epi_step, step(b, EDGE_ADDED))
                dve.tensor_tensor(summed[:], summed[:], x_rows[:], ALU.add).then_inc(epi_step, 1)

            def mean_and_var(b):
                dve.wait_ge(epi_step, step(b, RESIDUAL_ADDED))
                for s in range(SUBS):
                    last = dve.bn_stats(stats[:, s], summed[:, s])
                last.then_inc(epi_step, 1)
                dve.drain()
                for s in range(SUBS):
                    last = dve.bn_aggr(mean_var[:, s], stats[:, s])
                last.then_inc(epi_step, 1)

            def normalise(b):
                dve.wait_ge(std_ready, b + 1)
                dve.reciprocal(rstd[:], std[:]).then_inc(epi_step, 1)
                dve.wait_ge(epi_step, step(b, RSTD))
                for s in range(SUBS):
                    last = dve.tensor_scalar(normed[:, s], summed[:, s], mean_var[:, s, 0:1], rstd[:, s:s + 1],
                                             ALU.subtract, ALU.mult)
                last.then_inc(epi_step, 1)

            for n in range(X_LOADS):
                dve.wait_ge(raw_loaded[n], 16)
                dve.wait_ge(hi_ready, n + 1)
                dve.tensor_tensor(x_lo[:, n * WIDE:(n + 1) * WIDE], raw[:, n],
                                  x_hi[:, n * WIDE:(n + 1) * WIDE].bitcast(F32), ALU.subtract).then_inc(lo_ready, 1)
            dve.wait_ge(weights_loaded, 5 * 16)

            for u in range(UNITS):
                dve.wait_ge(raw_loaded[u % RAW_RING], arrived(0, u))
                if u >= POS_RING:
                    dve.wait_ge(pos_used, units(0, u - POS_RING))
                mask_positive(u)
                split_unit(0, u)
            with dve.Fori(1, BLOCKS) as b:
                for u in range(UNITS):
                    if u == POS_RING - 1:
                        evict_pos(b - 1)
                    dve.wait_ge(raw_loaded[u % RAW_RING], arrived(b, u))
                    dve.wait_ge(pos_used, units(b, u - POS_RING))
                    mask_positive(u)
                    split_unit(b, u)
                    if u == SUM_AT:
                        add_up(b - 1, b - 1)
                    if u == STATS_AT:
                        mean_and_var(b - 1)
                    if u == NORM_AT:
                        normalise(b - 1)
                dve.wait_ge(stored, b * 16)
            evict_pos(BLOCKS - 1)
            add_up(BLOCKS - 1, BLOCKS - 1)
            mean_and_var(BLOCKS - 1)
            normalise(BLOCKS - 1)

            dve.wait_ge(hi_ready, split(BLOCKS - 1, UNITS - 1))
            dve.reduce_sum(neg_total[:], neg_sums[:], AX.X).then_inc(summed_up, 1)
            dve.wait_ge(total_ready, 1)
            dve.tensor_scalar(none_negative[:], total_ps[:], 0.0, None, ALU.is_equal).then_inc(flag_ready, 1)

            dve.wait_ge(flag_ready, 1)
            with dve.If(dve.value_load(none_negative[0:1, 0:1]) == 0):
                with dve.Fori(BLOCKS, 2 * BLOCKS) as b:
                    for u in range(UNITS):
                        dve.wait_ge(raw_loaded[u % RAW_RING], arrived(b, u))
                        dve.wait_ge(pos_used, units(b, u - POS_RING))
                        mask_positive(u)
                        mask_negative(u)
                        split_unit(b, u)
                        dve.wait_ge(neg_used, units(b - BLOCKS, u))
                    evict_pos(b)
                    dve.tensor_copy(neg_support[:], neg_ps[:]).then_inc(neg_evicted, 1)
                    dve.wait_ge(stored, b * 16)
                    add_up(b, b - BLOCKS)
                    mean_and_var(b)
                    normalise(b)

        @block.tensor
        def _(pe):
            def times_mask(mask, out_ps, u, used):
                for t in range(TILES):
                    first, last = (u, t) == (0, 0), (u, t) == (UNITS - 1, TILES - 1)
                    pe.matmul(out_ps[:], x_tile(x_hi, u, t), mask[:, tile(t)], start=first, stop=False)
                    mm = pe.matmul(out_ps[:], x_tile(x_lo, u, t), mask[:, tile(t)], start=False, stop=last)
                mm.then_inc(used, 1)

            def times_adj(u):
                hi, lo = adj_hi[:, u % SPLIT_RING], adj_lo[:, u % SPLIT_RING]
                for t in range(TILES):
                    first, last = (u, t) == (0, 0), (u, t) == (UNITS - 1, TILES - 1)
                    pe.matmul(edge_ps[:], x_tile(x_hi, u, t), hi[:, tile(t)], start=first, stop=False)
                    pe.matmul(edge_ps[:], x_tile(x_hi, u, t), lo[:, tile(t)], start=False, stop=False)
                    mm = pe.matmul(edge_ps[:], x_tile(x_lo, u, t), hi[:, tile(t)], start=False, stop=last)
                mm.then_inc(split_used, 1)

            def unit(b, u, after_another):
                if after_another and u == 0:
                    pe.wait_ge(pos_evicted, b)
                pe.wait_ge(pos_ready, units(b, u))
                times_mask(pos[:, u % POS_RING], pos_ps, u, pos_used)
                if after_another and u == 0:
                    pe.wait_ge(edge_evicted, b)
                pe.wait_ge(lo_ready, split(b, u))
                times_adj(u)

            def project(b, with_neg):
                pe.wait_ge(pos_evicted, b + 1)
                pe.wait_ge(edge_evicted, b + 1)
                if with_neg:
                    pe.wait_ge(neg_evicted, b - (BLOCKS - 1))
                for s in range(SUBS):
                    rows = slice(s * P, (s + 1) * P)
                    pe.matmul(node_out_ps[:, s], pos_support[:, rows], w_pos_sb[:], start=True, stop=not with_neg)
                    if with_neg:
                        pe.matmul(node_out_ps[:, s], neg_support[:, rows], w_neg_sb[:], start=False, stop=True)
                    mm = pe.matmul(edge_out_ps[:, s], edge_support[:, rows], w_edge_sb[:], start=True, stop=True)
                mm.then_inc(projected, 1)

            for u in range(UNITS):
                if u * TILES % X_TILES == 0:
                    pe.wait_ge(lo_ready, u * TILES // X_TILES + 1)
                unit(0, u, False)
            pe.wait_ge(weights_loaded, 5 * 16)
            with pe.Fori(1, BLOCKS) as b:
                for u in range(UNITS):
                    unit(b, u, True)
                    if u == PROJECT_AT:
                        project(b - 1, False)
            project(BLOCKS - 1, False)

            pe.wait_ge(constants_set, 2)
            pe.wait_ge(summed_up, 1)
            pe.matmul(total_ps[:], neg_total[:], ones[:], start=True, stop=True).then_inc(total_ready, 1)

            pe.wait_ge(flag_ready, 1)
            with pe.If(pe.value_load(none_negative[0:1, 0:1]) == 0):
                with pe.Fori(BLOCKS, 2 * BLOCKS) as b:
                    for u in range(UNITS):
                        if u == 0:
                            pe.wait_ge(pos_evicted, b)
                        pe.wait_ge(pos_ready, units(b, u))
                        times_mask(pos[:, u % POS_RING], pos_ps, u, pos_used)
                        pe.wait_ge(neg_ready, units(b - BLOCKS, u))
                        times_mask(neg, neg_ps, u, neg_used)
                        if u == 0:
                            pe.wait_ge(edge_evicted, b)
                        pe.wait_ge(lo_ready, split(b, u))
                        times_adj(u)
                    project(b, True)


def kernel(x, adj, L0_gnn_node_weight, L0_gnn_node_bias, L0_gnn_edge_weight, L0_gnn_edge_bias):
    import concourse.bacc as bacc
    from concourse.bass_utils import run_bass_kernel_spmd

    N, F = x.shape
    blocks, units = N // COLS, N // (TILES * P)
    arrays = {
        "adj": np.ascontiguousarray(
            np.asarray(adj).reshape(blocks, COLS, units, TILES, P).transpose(0, 2, 4, 3, 1)
        ).reshape(blocks, units, P, WIDE),
        "x": np.ascontiguousarray(np.asarray(x).reshape(N // P, P, F).transpose(1, 0, 2)).reshape(P, N // P * F),
        "w_node": np.ascontiguousarray(L0_gnn_node_weight),
        "b_node": np.ascontiguousarray(L0_gnn_node_bias),
        "w_edge": np.ascontiguousarray(L0_gnn_edge_weight),
        "b_edge": np.ascontiguousarray(L0_gnn_edge_bias),
    }
    nc = bacc.Bacc("TRN2", target_bir_lowering=False, num_devices=1)
    args = [nc.dram_tensor(n, a.shape, F32, kind="ExternalInput").ap() for n, a in arrays.items()]
    out = nc.dram_tensor("out", (blocks, P, COLS // P * F), F32, kind="ExternalOutput").ap()
    adj_resnorm(nc, *args, out)
    result = run_bass_kernel_spmd(nc, [arrays], core_ids=[0]).results[0]["out"]
    return np.ascontiguousarray(result.reshape(blocks, P, COLS // P, F).transpose(0, 2, 1, 3)).reshape(N, F)
```

```python
from contextlib import ExitStack

import numpy as np

import concourse.bass as bass
from concourse import mybir

F32 = mybir.dt.float32
F32R = mybir.dt.float32r
BF16 = mybir.dt.bfloat16
I32 = mybir.dt.int32
ALU = mybir.AluOpType
ACT = mybir.ActivationFunctionType
AX = mybir.AxisListType

P = 128
COLS = 512
TILES = 4
WIDE = TILES * COLS
X_WIDE = WIDE // 2
RAW_RING = 4
SPLIT_RING = 4
POS_RING = 2
EPS = 1e-5
NEG_SCALE = -(2.0 ** 64)

X_ROWS, X_BIASED, NODE_BIASED, NODE_ADDED, EDGE_ADDED, MEAN_VAR, RSTD, NORMED = range(1, 9)
EPI_STEPS = NORMED

X_LEAD = 1

EVICT_EDGE_AT, PROJECT_AT, SUM_AT, STATS_AT, SQRT_AT, NORM_AT, STORE_AT = 2, 1, 5, 6, 7, 8, 12


def adj_resnorm(nc, adj, x, w_node, b_node, w_edge, b_edge, out):
    BLOCKS, UNITS = adj.shape[0], adj.shape[1]
    F = w_edge.shape[0]
    SUBS = COLS // P
    X_LOADS = x.shape[1] // X_WIDE
    X_SPAN = UNITS // X_LOADS
    ROUNDS = UNITS // RAW_RING
    assert X_LOADS % RAW_RING == 0 and SUBS * F == COLS
    assert UNITS % RAW_RING == 0 and UNITS % SPLIT_RING == 0 and UNITS % POS_RING == 0

    with ExitStack() as stack:
        def sbuf(name, shape, dtype):
            return stack.enter_context(nc.sbuf_tensor(name, shape, dtype))

        def psum(name, shape, dtype):
            return stack.enter_context(nc.psum_tensor(name, shape, dtype))

        def semaphore(name):
            return stack.enter_context(nc.semaphore(name))

        x_hi = sbuf("x_hi", [P, x.shape[1]], F32R)
        x_lo = sbuf("x_lo", [P, x.shape[1]], F32R)
        raw = sbuf("raw", [P, RAW_RING, WIDE], F32)
        adj_hi = sbuf("adj_hi", [P, SPLIT_RING, WIDE], F32R)
        adj_lo = sbuf("adj_lo", [P, SPLIT_RING, WIDE], F32R)
        pos = sbuf("pos", [P, POS_RING, WIDE], F32R)
        neg = sbuf("neg", [P, WIDE], F32R)
        relu_out = sbuf("relu_out", [P, 2, WIDE], BF16)
        neg_sums = sbuf("neg_sums", [P, BLOCKS * UNITS], F32)
        neg_total = sbuf("neg_total", [P, 1], F32)
        ones = sbuf("ones", [P, 1], F32)
        none_negative = sbuf("none_negative", [1, 1], I32)
        pos_support = sbuf("pos_support", [P, COLS], F32)
        neg_support = sbuf("neg_support", [P, COLS], F32)
        edge_support = sbuf("edge_support", [P, COLS], F32)
        w_pos_sb = sbuf("w_pos_sb", [P, F], F32)
        w_neg_sb = sbuf("w_neg_sb", [P, F], F32)
        w_edge_sb = sbuf("w_edge_sb", [P, F], F32)
        b_node_sb = sbuf("b_node_sb", [P, F], F32)
        b_edge_sb = sbuf("b_edge_sb", [P, F], F32)
        eps_sb = sbuf("eps_sb", [P, 1], F32)
        x_rows = sbuf("x_rows", [P, SUBS, F], F32)
        summed = sbuf("summed", [P, SUBS, F], F32)
        normed = sbuf("normed", [P, SUBS, F], F32)
        stats = sbuf("stats", [P, SUBS, 6], F32)
        mean_var = sbuf("mean_var", [P, SUBS, 2], F32)
        std = sbuf("std", [P, SUBS], F32)
        rstd = sbuf("rstd", [P, SUBS], F32)
        pos_ps = psum("pos_ps", [P, COLS], F32)
        neg_ps = psum("neg_ps", [P, COLS], F32)
        edge_ps = psum("edge_ps", [P, COLS], F32)
        node_out_ps = psum("node_out_ps", [P, SUBS, F], F32)
        edge_out_ps = psum("edge_out_ps", [P, SUBS, F], F32)
        total_ps = psum("total_ps", [1, 1], F32)
        raw_loaded = [semaphore(f"raw_loaded_{slot}") for slot in range(RAW_RING)]
        weights_loaded = semaphore("weights_loaded")
        constants_set = semaphore("constants_set")
        x_rounded = semaphore("x_rounded")
        hi_ready = semaphore("hi_ready")
        lo_ready = semaphore("lo_ready")
        pos_ready = semaphore("pos_ready")
        neg_ready = semaphore("neg_ready")
        pos_used = semaphore("pos_used")
        neg_used = semaphore("neg_used")
        split_used = semaphore("split_used")
        pos_evicted = semaphore("pos_evicted")
        neg_evicted = semaphore("neg_evicted")
        edge_evicted = semaphore("edge_evicted")
        node_projected = semaphore("node_projected")
        edge_projected = semaphore("edge_projected")
        epi_step = semaphore("epi_step")
        std_ready = semaphore("std_ready")
        stored = semaphore("stored")
        summed_up = semaphore("summed_up")
        total_ready = semaphore("total_ready")
        flag_ready = semaphore("flag_ready")

        block = stack.enter_context(nc.Block())

        opening = []
        for u in range(UNITS):
            if u == 0 or (u + X_LEAD) % X_SPAN == 0 and u + X_LEAD < UNITS:
                opening.append(("x", (u + X_LEAD) // X_SPAN))
            opening.append(("adj", u))

        def arrived(b, u):
            return b * (16 * ROUNDS) + 16 * (u // RAW_RING + 1 + X_LOADS // RAW_RING)

        def units(b, u):
            return b * UNITS + (u + 1)

        def split(b, u):
            return b * UNITS + (X_LOADS + u + 1)

        def step(b, s):
            return b * EPI_STEPS + s

        def tile(t):
            return slice(t * COLS, (t + 1) * COLS)

        def x_tile(xs, u, t):
            k = u * TILES + t
            return xs[:, k * F:(k + 1) * F]

        @block.sync
        def _(sp):
            def load_unit(b, src, u):
                sp.wait_ge(lo_ready, split(b, u - RAW_RING))
                sp.dma_start(raw[:, u % RAW_RING], adj[src, u]).then_inc(raw_loaded[u % RAW_RING], 16)

            def store_block(b, dst):
                sp.wait_ge(epi_step, step(b, NORMED))
                sp.dma_start(out[dst], normed[:].rearrange("p s f -> p (s f)")).then_inc(stored, 16)

            for n, (what, i) in enumerate(opening):
                if n >= RAW_RING:
                    sp.wait_ge(lo_ready, n - RAW_RING + 1)
                src, dst = (adj[0, i], raw[:, n % RAW_RING]) if what == "adj" else (
                    x[:, i * X_WIDE:(i + 1) * X_WIDE], raw[:, n % RAW_RING, 0:X_WIDE])
                sp.dma_start(dst, src).then_inc(raw_loaded[n % RAW_RING], 16)
            with sp.Fori(1, BLOCKS) as b:
                for u in range(UNITS):
                    load_unit(b, b, u)
                    if u == STORE_AT:
                        store_block(b - 1, b - 1)
            store_block(BLOCKS - 1, BLOCKS - 1)

            sp.wait_ge(flag_ready, 1)
            with sp.If(sp.value_load(none_negative[0:1, 0:1]) == 0):
                with sp.Fori(BLOCKS, 2 * BLOCKS) as b:
                    for u in range(UNITS):
                        load_unit(b, b - BLOCKS, u)
                    store_block(b, b - BLOCKS)
                sp.wait_ge(stored, 2 * BLOCKS * 16)
            with sp.Else():
                sp.wait_ge(stored, BLOCKS * 16)

        @block.gpsimd
        def _(pool):
            pool.memset(eps_sb[:], EPS).then_inc(constants_set, 1)
            pool.memset(ones[:], 1.0).then_inc(constants_set, 1)
            pool.dma_start(w_pos_sb[:], w_node[0:F, :]).then_inc(weights_loaded, 16)
            pool.dma_start(w_neg_sb[:], w_node[F:2 * F, :]).then_inc(weights_loaded, 16)
            pool.dma_start(w_edge_sb[:], w_edge).then_inc(weights_loaded, 16)
            pool.dma_start(b_node_sb[:], b_node.partition_broadcast(P)).then_inc(weights_loaded, 16)
            pool.dma_start(b_edge_sb[:], b_edge.partition_broadcast(P)).then_inc(weights_loaded, 16)

        @block.scalar
        def _(act):
            def add_up_negatives(b, u, slot):
                act.activation(relu_out[:, u % 2], raw[:, slot], ACT.Relu, scale=NEG_SCALE,
                               accum_out=neg_sums[:, bass.ds(b * UNITS + u, 1)])

            def round_unit(u, slot):
                act.activation(adj_hi[:, u % SPLIT_RING], raw[:, slot], ACT.Copy).then_inc(hi_ready, 1)

            def evict_edge(b):
                act.wait_ge(split_used, units(b, UNITS - 1))
                act.activation(edge_support[:], edge_ps[:], ACT.Copy).then_inc(edge_evicted, 1)

            def sqrt_var(b):
                act.wait_ge(epi_step, step(b, MEAN_VAR))
                act.activation(std[:], mean_var[:, :, 1], ACT.Sqrt, bias=eps_sb[:]).then_inc(std_ready, 1)

            act.wait_ge(constants_set, 2)
            act.activation(std[:, 0:1], eps_sb[:], ACT.Sqrt)
            for n, (what, i) in enumerate(opening):
                if what == "x":
                    continue
                act.wait_ge(raw_loaded[n % RAW_RING], 16 * (n // RAW_RING + 1))
                if i >= 2:
                    act.wait_ge(hi_ready, units(0, i - 2))
                add_up_negatives(0, i, n % RAW_RING)
                if i >= SPLIT_RING:
                    act.wait_ge(split_used, units(0, i - SPLIT_RING))
                round_unit(i, n % RAW_RING)
            with act.Fori(1, BLOCKS) as b:
                for u in range(UNITS):
                    act.wait_ge(raw_loaded[u % RAW_RING], arrived(b, u))
                    act.wait_ge(hi_ready, units(b, u - 2))
                    add_up_negatives(b, u, u % RAW_RING)
                    if u == EVICT_EDGE_AT:
                        evict_edge(b - 1)
                    act.wait_ge(split_used, units(b, u - SPLIT_RING))
                    round_unit(u, u % RAW_RING)
                    if u == SQRT_AT:
                        sqrt_var(b - 1)
            evict_edge(BLOCKS - 1)
            sqrt_var(BLOCKS - 1)

            act.wait_ge(flag_ready, 1)
            with act.If(act.value_load(none_negative[0:1, 0:1]) == 0):
                with act.Fori(BLOCKS, 2 * BLOCKS) as b:
                    for u in range(UNITS):
                        act.wait_ge(raw_loaded[u % RAW_RING], arrived(b, u))
                        act.wait_ge(split_used, units(b, u - SPLIT_RING))
                        round_unit(u, u % RAW_RING)
                    evict_edge(b)
                    sqrt_var(b)

        @block.vector
        def _(dve):
            def mask_positive(u, slot):
                dve.tensor_scalar(pos[:, u % POS_RING], raw[:, slot], 0.0, None, ALU.is_gt).then_inc(pos_ready, 1)

            def mask_negative(slot):
                dve.tensor_scalar(neg[:], raw[:, slot], 0.0, None, ALU.is_lt).then_inc(neg_ready, 1)

            def split_unit(u, slot):
                dve.tensor_tensor(adj_lo[:, u % SPLIT_RING], raw[:, slot],
                                  adj_hi[:, u % SPLIT_RING].bitcast(F32), ALU.subtract).then_inc(lo_ready, 1)

            def evict_pos(b):
                dve.wait_ge(pos_used, units(b, UNITS - 1))
                dve.tensor_copy(pos_support[:], pos_ps[:]).then_inc(pos_evicted, 1)

            def as_rows(xs, rows):
                return xs[:, bass.ds(rows * COLS, COLS)].bitcast(F32).rearrange("p (s f) -> p s f", f=F)

            def add_up(b, rows):
                dve.tensor_tensor(x_rows[:], as_rows(x_hi, rows), as_rows(x_lo, rows), ALU.add).then_inc(epi_step, 1)
                dve.wait_ge(epi_step, step(b, X_ROWS))
                dve.tensor_tensor(x_rows[:], x_rows[:], b_edge_sb[:].unsqueeze(1).broadcast_to([P, SUBS, F]),
                                  ALU.add).then_inc(epi_step, 1)
                dve.wait_ge(node_projected, b + 1)
                dve.tensor_tensor(summed[:], node_out_ps[:], b_node_sb[:].unsqueeze(1).broadcast_to([P, SUBS, F]),
                                  ALU.add).then_inc(epi_step, 1)
                dve.wait_ge(epi_step, step(b, NODE_BIASED))
                dve.scalar_tensor_tensor(summed[:], summed[:], 0.0, x_rows[:], ALU.max, ALU.add).then_inc(epi_step, 1)
                dve.wait_ge(epi_step, step(b, NODE_ADDED))
                dve.wait_ge(edge_projected, b + 1)
                dve.tensor_tensor(summed[:], summed[:], edge_out_ps[:], ALU.add).then_inc(epi_step, 1)

            def mean_and_var(b):
                dve.wait_ge(epi_step, step(b, EDGE_ADDED))
                for s in range(SUBS):
                    dve.bn_stats(stats[:, s], summed[:, s])
                dve.drain()
                for s in range(SUBS):
                    last = dve.bn_aggr(mean_var[:, s], stats[:, s])
                last.then_inc(epi_step, 1)

            def normalise(b):
                dve.wait_ge(std_ready, b + 1)
                dve.reciprocal(rstd[:], std[:]).then_inc(epi_step, 1)
                dve.wait_ge(epi_step, step(b, RSTD))
                for s in range(SUBS):
                    last = dve.tensor_scalar(normed[:, s], summed[:, s], mean_var[:, s, 0:1], rstd[:, s:s + 1],
                                             ALU.subtract, ALU.mult)
                last.then_inc(epi_step, 1)

            for n, (what, i) in enumerate(opening):
                slot = n % RAW_RING
                dve.wait_ge(raw_loaded[slot], 16 * (n // RAW_RING + 1))
                if what == "x":
                    cols, loaded = slice(i * X_WIDE, (i + 1) * X_WIDE), raw[:, slot, 0:X_WIDE]
                    dve.tensor_copy(x_hi[:, cols], loaded).then_inc(x_rounded, 1)
                    dve.wait_ge(x_rounded, i + 1)
                    dve.tensor_tensor(x_lo[:, cols], loaded, x_hi[:, cols].bitcast(F32), ALU.subtract).then_inc(lo_ready, 1)
                    continue
                if i >= POS_RING:
                    dve.wait_ge(pos_used, units(0, i - POS_RING))
                mask_positive(i, slot)
                dve.wait_ge(hi_ready, units(0, i))
                split_unit(i, slot)
            dve.wait_ge(weights_loaded, 5 * 16)
            with dve.Fori(1, BLOCKS) as b:
                for u in range(UNITS):
                    if u == POS_RING - 1:
                        evict_pos(b - 1)
                    dve.wait_ge(raw_loaded[u % RAW_RING], arrived(b, u))
                    dve.wait_ge(pos_used, units(b, u - POS_RING))
                    mask_positive(u, u % RAW_RING)
                    dve.wait_ge(hi_ready, units(b, u))
                    split_unit(u, u % RAW_RING)
                    if u == SUM_AT:
                        add_up(b - 1, b - 1)
                    if u == STATS_AT:
                        mean_and_var(b - 1)
                    if u == NORM_AT:
                        normalise(b - 1)
                dve.wait_ge(stored, b * 16)

            dve.wait_ge(hi_ready, units(BLOCKS - 1, UNITS - 1))
            dve.reduce_sum(neg_total[:], neg_sums[:], AX.X).then_inc(summed_up, 1)
            evict_pos(BLOCKS - 1)
            add_up(BLOCKS - 1, BLOCKS - 1)
            mean_and_var(BLOCKS - 1)
            normalise(BLOCKS - 1)
            dve.wait_ge(total_ready, 1)
            dve.tensor_scalar(none_negative[:], total_ps[:], 0.0, None, ALU.is_equal).then_inc(flag_ready, 1)

            dve.wait_ge(flag_ready, 1)
            with dve.If(dve.value_load(none_negative[0:1, 0:1]) == 0):
                with dve.Fori(BLOCKS, 2 * BLOCKS) as b:
                    for u in range(UNITS):
                        dve.wait_ge(raw_loaded[u % RAW_RING], arrived(b, u))
                        dve.wait_ge(pos_used, units(b, u - POS_RING))
                        mask_positive(u, u % RAW_RING)
                        mask_negative(u % RAW_RING)
                        dve.wait_ge(hi_ready, units(b, u))
                        split_unit(u, u % RAW_RING)
                        dve.wait_ge(neg_used, units(b - BLOCKS, u))
                    evict_pos(b)
                    dve.tensor_copy(neg_support[:], neg_ps[:]).then_inc(neg_evicted, 1)
                    dve.wait_ge(stored, b * 16)
                    add_up(b, b - BLOCKS)
                    mean_and_var(b)
                    normalise(b)

        @block.tensor
        def _(pe):
            def times_mask(mask, out_ps, u, used):
                for t in range(TILES):
                    first, last = (u, t) == (0, 0), (u, t) == (UNITS - 1, TILES - 1)
                    pe.matmul(out_ps[:], x_tile(x_hi, u, t), mask[:, tile(t)], start=first, stop=False)
                    mm = pe.matmul(out_ps[:], x_tile(x_lo, u, t), mask[:, tile(t)], start=False, stop=last)
                mm.then_inc(used, 1)

            def times_adj(u):
                hi, lo = adj_hi[:, u % SPLIT_RING], adj_lo[:, u % SPLIT_RING]
                for t in range(TILES):
                    first, last = (u, t) == (0, 0), (u, t) == (UNITS - 1, TILES - 1)
                    pe.matmul(edge_ps[:], x_tile(x_hi, u, t), hi[:, tile(t)], start=first, stop=False)
                    pe.matmul(edge_ps[:], x_tile(x_hi, u, t), lo[:, tile(t)], start=False, stop=False)
                    mm = pe.matmul(edge_ps[:], x_tile(x_lo, u, t), hi[:, tile(t)], start=False, stop=last)
                mm.then_inc(split_used, 1)

            def project(b, with_neg):
                pe.wait_ge(pos_evicted, b + 1)
                if with_neg:
                    pe.wait_ge(neg_evicted, b - (BLOCKS - 1))
                for s in range(SUBS):
                    rows = slice(s * P, (s + 1) * P)
                    mm = pe.matmul(node_out_ps[:, s], pos_support[:, rows], w_pos_sb[:], start=True, stop=not with_neg)
                    if with_neg:
                        mm = pe.matmul(node_out_ps[:, s], neg_support[:, rows], w_neg_sb[:], start=False, stop=True)
                mm.then_inc(node_projected, 1)
                pe.wait_ge(edge_evicted, b + 1)
                for s in range(SUBS):
                    rows = slice(s * P, (s + 1) * P)
                    mm = pe.matmul(edge_out_ps[:, s], edge_support[:, rows], w_edge_sb[:], start=True, stop=True)
                mm.then_inc(edge_projected, 1)

            for n, (what, u) in enumerate(opening):
                if what == "x":
                    pe.wait_ge(lo_ready, n + 1)
                    continue
                pe.wait_ge(pos_ready, units(0, u))
                times_mask(pos[:, u % POS_RING], pos_ps, u, pos_used)
                pe.wait_ge(lo_ready, n + 1)
                times_adj(u)
            pe.wait_ge(weights_loaded, 5 * 16)
            with pe.Fori(1, BLOCKS) as b:
                for u in range(UNITS):
                    if u == 0:
                        pe.wait_ge(pos_evicted, b)
                    pe.wait_ge(pos_ready, units(b, u))
                    times_mask(pos[:, u % POS_RING], pos_ps, u, pos_used)
                    if u == 0:
                        pe.wait_ge(edge_evicted, b)
                    pe.wait_ge(lo_ready, split(b, u))
                    times_adj(u)
                    if u == PROJECT_AT:
                        project(b - 1, False)

            pe.wait_ge(constants_set, 2)
            pe.wait_ge(summed_up, 1)
            pe.matmul(total_ps[:], neg_total[:], ones[:], start=True, stop=True).then_inc(total_ready, 1)
            project(BLOCKS - 1, False)

            pe.wait_ge(flag_ready, 1)
            with pe.If(pe.value_load(none_negative[0:1, 0:1]) == 0):
                with pe.Fori(BLOCKS, 2 * BLOCKS) as b:
                    for u in range(UNITS):
                        if u == 0:
                            pe.wait_ge(pos_evicted, b)
                        pe.wait_ge(pos_ready, units(b, u))
                        times_mask(pos[:, u % POS_RING], pos_ps, u, pos_used)
                        pe.wait_ge(neg_ready, units(b - BLOCKS, u))
                        times_mask(neg, neg_ps, u, neg_used)
                        if u == 0:
                            pe.wait_ge(edge_evicted, b)
                        pe.wait_ge(lo_ready, split(b, u))
                        times_adj(u)
                    project(b, True)


def kernel(x, adj, L0_gnn_node_weight, L0_gnn_node_bias, L0_gnn_edge_weight, L0_gnn_edge_bias):
    import concourse.bacc as bacc
    from concourse.bass_utils import run_bass_kernel_spmd

    N, F = x.shape
    blocks, units = N // COLS, N // (TILES * P)
    arrays = {
        "adj": np.ascontiguousarray(
            np.asarray(adj).reshape(blocks, COLS, units, TILES, P).transpose(0, 2, 4, 3, 1)
        ).reshape(blocks, units, P, WIDE),
        "x": np.ascontiguousarray(np.asarray(x).reshape(N // P, P, F).transpose(1, 0, 2)).reshape(P, N // P * F),
        "w_node": np.ascontiguousarray(L0_gnn_node_weight),
        "b_node": np.ascontiguousarray(L0_gnn_node_bias),
        "w_edge": np.ascontiguousarray(L0_gnn_edge_weight),
        "b_edge": np.ascontiguousarray(L0_gnn_edge_bias),
    }
    nc = bacc.Bacc("TRN2", target_bir_lowering=False, num_devices=1)
    args = [nc.dram_tensor(n, a.shape, F32, kind="ExternalInput").ap() for n, a in arrays.items()]
    out = nc.dram_tensor("out", (blocks, P, COLS // P * F), F32, kind="ExternalOutput").ap()
    adj_resnorm(nc, *args, out)
    result = run_bass_kernel_spmd(nc, [arrays], core_ids=[0]).results[0]["out"]
    return np.ascontiguousarray(result.reshape(blocks, P, COLS // P, F).transpose(0, 2, 1, 3)).reshape(N, F)
```
